# Optimizing a Trainium2 kernel written in Bass

```python
import numpy as np
import jax
import jax.numpy as jnp

def _softmax(x, axis=-1):
    return jax.nn.softmax(x, axis=axis)

def _gelu(x):
    return jax.nn.gelu(x, approximate=True)

def _silu(x):
    return jax.nn.silu(x)

def _sigmoid(x):
    return jax.nn.sigmoid(x)

def _layernorm(x, axis=-1, eps=1e-05):
    m = jnp.mean(x, axis=axis, keepdims=True)
    v = jnp.var(x, axis=axis, keepdims=True)
    return (x - m) / jnp.sqrt(v + eps)

def _scatter_add(tgt, idx, src, axis=0):
    return tgt.at[idx].add(src)

def _segment_sum(src, seg, n):
    return jax.ops.segment_sum(src, seg, n)
kernel_name = 'mk_seq_postln_d1_jaxref_r8_6734e9'

def setup_inputs(seed: int=0):
    np.random.seed(seed)
    _w = jnp.asarray

    def _L0_attn_setup():
        import math
        import jax, jax.numpy as jnp
        import numpy as np
        B, T, C = (2, 256, 128)
        HEADS = 16
        HD = C // HEADS

        def _rope_tables(seq_len, dim):
            pos = jnp.arange(seq_len, dtype=jnp.float32)
            freqs = 1.0 / 10000.0 ** (jnp.arange(0, dim, 2, dtype=jnp.float32) / dim)
            ang = pos[:, None] * freqs[None, :]
            return (jnp.sin(ang)[None, :, None, :], jnp.cos(ang)[None, :, None, :])

        def _apply_rope(t, sin, cos, dim):
            t1, t2 = (t[..., :dim // 2], t[..., dim // 2:])
            return jnp.concatenate([t1 * cos + t2 * sin, t1 * sin - t2 * cos], axis=-1)
        key = jax.random.key(seed)
        ks = jax.random.split(key, 5)
        s = 0.02
        return {'x': jax.random.normal(ks[0], (B, T, C), jnp.float32), 'Wq': jax.random.normal(ks[1], (C, C), jnp.float32) * s, 'bq': jnp.zeros((C,), jnp.float32), 'Wk': jax.random.normal(ks[2], (C, HD), jnp.float32) * s, 'bk': jnp.zeros((HD,), jnp.float32), 'Wv': jax.random.normal(ks[3], (C, HD), jnp.float32) * s, 'bv': jnp.zeros((HD,), jnp.float32), 'Wo': jax.random.normal(ks[4], (C, C), jnp.float32) * s, 'bo': jnp.zeros((C,), jnp.float32)}
    _L0_attn_in = _L0_attn_setup()

    def _L0_ffn_setup():
        import jax, jax.numpy as jnp
        import numpy as np
        D = 128
        HQ = 16
        HKV = 4
        G = HQ // HKV
        K = 64
        V = 64
        E = 8
        TOPK = 2
        HID = 256
        CAP_FRAC = 0.125
        EPS = 1e-06

        def _rmsnorm(x, g):
            return x * jax.lax.rsqrt(jnp.mean(x * x, axis=-1, keepdims=True) + EPS) * g

        def _rotary_tables(t, dim):
            thetas = 10000.0 ** (-np.arange(0, dim, 2, dtype=np.float32) / dim)
            ticks = np.outer(np.arange(t, dtype=np.float32), thetas)
            ticks = np.tile(ticks, (1, 2))[None, :, None, :]
            return (jnp.asarray(np.cos(ticks)), jnp.asarray(np.sin(ticks)))

        def _neg_half(x):
            x1, x2 = jnp.split(x, 2, axis=-1)
            return jnp.concatenate([-x2, x1], axis=-1)

        def _attention(x, wq, wk, wv, wo):
            b, t, _ = x.shape
            q = (x @ wq).reshape(b, t, HQ, K)
            k = (x @ wk).reshape(b, t, HKV, K)
            v = (x @ wv).reshape(b, t, HKV, V)
            cos, sin = _rotary_tables(t, K)
            q = q * cos + _neg_half(q) * sin
            k = k * cos + _neg_half(k) * sin
            qg = q.reshape(b, t, G, HKV, K)
            scores = jnp.einsum('btghk,bThk->bghtT', qg, k)
            mask = jnp.tril(jnp.ones((t, t), bool))
            scores = jnp.where(mask, scores, -jnp.inf) / np.float32(np.sqrt(K))
            p = jax.nn.softmax(scores, axis=-1)
            out = jnp.einsum('bghtT,bThv->btghv', p, v).reshape(b, t, HQ * V)
            return out @ wo

        def _moe(x, router_w, router_b, w1, w2, w3):
            b, t, d = x.shape
            n = b * t
            xf = x.reshape(n, d)
            logits = xf @ router_w + router_b
            vals, idx = jax.lax.top_k(logits, TOPK)
            scores = jax.nn.softmax(vals, axis=-1)
            cap = int(np.floor(n * CAP_FRAC))
            oh = jax.nn.one_hot(idx, E, dtype=jnp.float32)
            pos = jnp.cumsum(jnp.cumsum(oh, axis=0), axis=1).astype(jnp.int32)
            emask = oh * (pos < cap)
            tmask = jnp.sum(emask, axis=-1)
            assign = jnp.einsum('tke,e->tk', emask, jnp.arange(E, dtype=jnp.float32)).astype(jnp.int32)
            m = jnp.max(assign, axis=-1)

            def ff(w1e, w2e, w3e):
                h = jax.nn.gelu(xf @ w2e * (xf @ w1e), approximate=False)
                return h @ w3e
            y_all = jax.vmap(ff)(w1, w2, w3)
            y = y_all[m, jnp.arange(n)]
            slot = jnp.where(tmask[..., None] > 0, y[:, None, :], xf[:, None, :])
            out = jnp.einsum('tkD,tk->tD', slot, scores)
            return out.reshape(b, t, d)
        key = jax.random.key(seed)
        ks = jax.random.split(key, 10)
        w = lambda k, shape: jax.random.normal(k, shape, jnp.float32) * 0.02
        return {'x': jax.random.normal(ks[0], (4, 64, D), jnp.float32), 'g1': jnp.ones((D,), jnp.float32), 'g2': jnp.ones((D,), jnp.float32), 'wq': w(ks[1], (D, HQ * K)), 'wk': w(ks[2], (D, HKV * K)), 'wv': w(ks[3], (D, HKV * V)), 'wo': w(ks[4], (HQ * V, D)), 'router_w': w(ks[5], (D, E)), 'router_b': jnp.zeros((E,), jnp.float32), 'w1': w(ks[6], (E, D, HID)), 'w2': w(ks[7], (E, D, HID)), 'w3': w(ks[8], (E, HID, D))}
    _L0_ffn_in = _L0_ffn_setup()
    _d = {'L0_attn_x': _L0_attn_in['x'], 'L0_attn_Wq': _L0_attn_in['Wq'], 'L0_attn_bq': _L0_attn_in['bq'], 'L0_attn_Wk': _L0_attn_in['Wk'], 'L0_attn_bk': _L0_attn_in['bk'], 'L0_attn_Wv': _L0_attn_in['Wv'], 'L0_attn_bv': _L0_attn_in['bv'], 'L0_attn_Wo': _L0_attn_in['Wo'], 'L0_attn_bo': _L0_attn_in['bo'], 'L0_ffn_g1': _L0_ffn_in['g1'], 'L0_ffn_g2': _L0_ffn_in['g2'], 'L0_ffn_wq': _L0_ffn_in['wq'], 'L0_ffn_wk': _L0_ffn_in['wk'], 'L0_ffn_wv': _L0_ffn_in['wv'], 'L0_ffn_wo': _L0_ffn_in['wo'], 'L0_ffn_router_w': _L0_ffn_in['router_w'], 'L0_ffn_router_b': _L0_ffn_in['router_b'], 'L0_ffn_w1': _L0_ffn_in['w1'], 'L0_ffn_w2': _L0_ffn_in['w2'], 'L0_ffn_w3': _L0_ffn_in['w3']}
    _x0 = _d['L0_attn_x']
    _d['L0_attn_x'] = jax.random.normal(jax.random.fold_in(jax.random.key(seed), 1), (8, 256, 128), dtype=_x0.dtype)
    del _x0
    return _d

def reference(L0_attn_x, L0_attn_Wq, L0_attn_bq, L0_attn_Wk, L0_attn_bk, L0_attn_Wv, L0_attn_bv, L0_attn_Wo, L0_attn_bo, L0_ffn_g1, L0_ffn_g2, L0_ffn_wq, L0_ffn_wk, L0_ffn_wv, L0_ffn_wo, L0_ffn_router_w, L0_ffn_router_b, L0_ffn_w1, L0_ffn_w2, L0_ffn_w3):

    def _L0_attn_ref(x, Wq, bq, Wk, bk, Wv, bv, Wo, bo):
        import math
        import jax, jax.numpy as jnp
        import numpy as np
        B, T, C = (2, 256, 128)
        HEADS = 16
        HD = C // HEADS

        def _rope_tables(seq_len, dim):
            pos = jnp.arange(seq_len, dtype=jnp.float32)
            freqs = 1.0 / 10000.0 ** (jnp.arange(0, dim, 2, dtype=jnp.float32) / dim)
            ang = pos[:, None] * freqs[None, :]
            return (jnp.sin(ang)[None, :, None, :], jnp.cos(ang)[None, :, None, :])

        def _apply_rope(t, sin, cos, dim):
            t1, t2 = (t[..., :dim // 2], t[..., dim // 2:])
            return jnp.concatenate([t1 * cos + t2 * sin, t1 * sin - t2 * cos], axis=-1)
        Bx, Tx, Cx = x.shape
        q = (x @ Wq + bq).reshape(Bx, Tx, HEADS, HD)
        k = (x @ Wk + bk)[:, :, None, :]
        v = (x @ Wv + bv)[:, :, None, :]
        sin, cos = _rope_tables(Tx, HD)
        q = _apply_rope(q, sin, cos, HD)
        k = _apply_rope(k, sin, cos, HD)
        att = jnp.einsum('bthd,bThd->bhtT', q, k) / math.sqrt(HD)
        causal = jnp.triu(jnp.ones((Tx, Tx), bool), 1)
        att = jnp.where(causal, -jnp.inf, att)
        att = jax.nn.softmax(att, axis=-1)
        out = jnp.einsum('bhtT,bThd->bthd', att, v).reshape(Bx, Tx, Cx)
        return out @ Wo + bo

    def _L0_ffn_ref(x, g1, g2, wq, wk, wv, wo, router_w, router_b, w1, w2, w3):
        import jax, jax.numpy as jnp
        import numpy as np
        D = 128
        HQ = 16
        HKV = 4
        G = HQ // HKV
        K = 64
        V = 64
        E = 8
        TOPK = 2
        HID = 256
        CAP_FRAC = 0.125
        EPS = 1e-06

        def _rmsnorm(x, g):
            return x * jax.lax.rsqrt(jnp.mean(x * x, axis=-1, keepdims=True) + EPS) * g

        def _rotary_tables(t, dim):
            thetas = 10000.0 ** (-np.arange(0, dim, 2, dtype=np.float32) / dim)
            ticks = np.outer(np.arange(t, dtype=np.float32), thetas)
            ticks = np.tile(ticks, (1, 2))[None, :, None, :]
            return (jnp.asarray(np.cos(ticks)), jnp.asarray(np.sin(ticks)))

        def _neg_half(x):
            x1, x2 = jnp.split(x, 2, axis=-1)
            return jnp.concatenate([-x2, x1], axis=-1)

        def _attention(x, wq, wk, wv, wo):
            b, t, _ = x.shape
            q = (x @ wq).reshape(b, t, HQ, K)
            k = (x @ wk).reshape(b, t, HKV, K)
            v = (x @ wv).reshape(b, t, HKV, V)
            cos, sin = _rotary_tables(t, K)
            q = q * cos + _neg_half(q) * sin
            k = k * cos + _neg_half(k) * sin
            qg = q.reshape(b, t, G, HKV, K)
            scores = jnp.einsum('btghk,bThk->bghtT', qg, k)
            mask = jnp.tril(jnp.ones((t, t), bool))
            scores = jnp.where(mask, scores, -jnp.inf) / np.float32(np.sqrt(K))
            p = jax.nn.softmax(scores, axis=-1)
            out = jnp.einsum('bghtT,bThv->btghv', p, v).reshape(b, t, HQ * V)
            return out @ wo

        def _moe(x, router_w, router_b, w1, w2, w3):
            b, t, d = x.shape
            n = b * t
            xf = x.reshape(n, d)
            logits = xf @ router_w + router_b
            vals, idx = jax.lax.top_k(logits, TOPK)
            scores = jax.nn.softmax(vals, axis=-1)
            cap = int(np.floor(n * CAP_FRAC))
            oh = jax.nn.one_hot(idx, E, dtype=jnp.float32)
            pos = jnp.cumsum(jnp.cumsum(oh, axis=0), axis=1).astype(jnp.int32)
            emask = oh * (pos < cap)
            tmask = jnp.sum(emask, axis=-1)
            assign = jnp.einsum('tke,e->tk', emask, jnp.arange(E, dtype=jnp.float32)).astype(jnp.int32)
            m = jnp.max(assign, axis=-1)

            def ff(w1e, w2e, w3e):
                h = jax.nn.gelu(xf @ w2e * (xf @ w1e), approximate=False)
                return h @ w3e
            y_all = jax.vmap(ff)(w1, w2, w3)
            y = y_all[m, jnp.arange(n)]
            slot = jnp.where(tmask[..., None] > 0, y[:, None, :], xf[:, None, :])
            out = jnp.einsum('tkD,tk->tD', slot, scores)
            return out.reshape(b, t, d)
        h = x + _attention(_rmsnorm(x, g1), wq, wk, wv, wo)
        return h + _moe(_rmsnorm(h, g2), router_w, router_b, w1, w2, w3)
    x = L0_attn_x
    x = _layernorm(x + _L0_attn_ref(x, L0_attn_Wq, L0_attn_bq, L0_attn_Wk, L0_attn_bk, L0_attn_Wv, L0_attn_bv, L0_attn_Wo, L0_attn_bo), axis=-1)
    x = _layernorm(x + _L0_ffn_ref(x, L0_ffn_g1, L0_ffn_g2, L0_ffn_wq, L0_ffn_wk, L0_ffn_wv, L0_ffn_wo, L0_ffn_router_w, L0_ffn_router_b, L0_ffn_w1, L0_ffn_w2, L0_ffn_w3), axis=-1)
    return x

_drawn_inputs = setup_inputs


def setup_inputs(seed=0):
    import zlib

    import numpy as np

    out = dict(_drawn_inputs(seed))
    spreads = {'L0_attn_bq': (0.0, 0.8),
     'L0_attn_bk': (0.0, 0.8),
     'L0_attn_bv': (0.0, 0.311),
     'L0_attn_bo': (0.0, 0.1),
     'L0_ffn_g1': (1.0, 0.6),
     'L0_ffn_g2': (1.0, 0.2),
     'L0_ffn_router_b': (0.0, 0.493)}
    factors = {'L0_attn_Wq': 8.0,
     'L0_attn_Wk': 8.0,
     'L0_attn_Wv': 7.423,
     'L0_ffn_wq': 8.0,
     'L0_ffn_wk': 8.0,
     'L0_ffn_wv': 3.392,
     'L0_ffn_wo': 3.665,
     'L0_ffn_router_w': 4.01,
     'L0_ffn_w1': 8.0,
     'L0_ffn_w2': 8.0,
     'L0_ffn_w3': 8.0}
    for name, (base, spread) in spreads.items():
        noise = np.random.default_rng([zlib.crc32(name.encode()), seed]).standard_normal(out[name].shape)
        drawn = base * np.exp(spread * noise) if base else spread * noise
        out[name] = jnp.asarray(drawn.astype(out[name].dtype))
    for name, factor in factors.items():
        out[name] = (out[name] * factor).astype(out[name].dtype)
    return out
```

```python
from contextlib import ExitStack

import numpy as np

import concourse.bass as bass
from concourse import mybir

F32 = mybir.dt.float32
F32R = mybir.dt.float32r
BF16 = mybir.dt.bfloat16
ALU = mybir.AluOpType
ACT = mybir.ActivationFunctionType
AX = mybir.AxisListType

P = 128
NB, T, C = 8, 256, 128
NT = T // P
NTILES = NB * NT
H = 16
DA = C // H
DB = 64
HKV = 4
G = H // HKV
E, HID = 8, 256
CAP = NB * T // E
EPS_LN, EPS_RMS = 1e-5, 1e-6
NEG = -1e30
NG = 512
QA = DA * (H + 1)
QB = (H + HKV) * DB

DIAG0, OFF, DIAG1 = 0, 1, 2
BLOCKS = {DIAG0: (0, 0), OFF: (0, 1), DIAG1: (1, 1)}
CHUNKS = [(DIAG0, 0), (DIAG0, 1), (OFF, 0), (DIAG1, 0), (OFF, 1), (DIAG1, 1)]
NCH = len(CHUNKS)

PM_A = [("P", "xT")] + [("M", f"m{i}") for i in range(6)] + [("P", "qkv")] \
    + [("M", f"m{i}") for i in range(6, 12)] + [("M", "nmT"), ("P", "qT"), ("P", "kT0"), ("P", "kT1")]
ST_A = [("S", "pv0"), ("T", "wo0"), ("T", "wo1"), ("S", "pv1")]
PM_B = [("M", f"m{i}") for i in range(4)] + [("P", "xT"), ("M", "m4"), ("M", "m5"), ("M", "m6"), ("M", "m7")] \
    + [("P", f"qkv0{i}") for i in range(3)] + [("M", "m8"), ("M", "m9")] \
    + [("P", f"qkv1{i}") for i in range(3)] + [("M", "m10"), ("M", "m11"), ("M", "nmT")] \
    + [("P", f"qkT{t}{i}") for t in range(NT) for i in range(3)]
ST_B = [("S", f"pv{i}") for i in range(6)] + [("T", "wo0"), ("T", "wo1"), ("S", "pv6"), ("S", "pv7"),
                                              ("T", "xfT"), ("T", "lg")]
AHEAD = {"P": 2, "M": 1, "S": 0, "T": -1}
FULL = 1


class Ring:

    def __init__(self, order, before=0):
        assert len(order) % 2 == 0
        self.order, self.before = order, before

    def active(self, step):
        return [use for stage, use in self.order if 0 <= step + AHEAD[stage] < NB]

    def index(self, step, use):
        at = step if isinstance(step, int) else FULL
        ahead = self.before + sum(len(self.active(i)) for i in range(-2, at))
        return ahead + self.active(at).index(use), 0 if isinstance(step, int) else step - FULL

    def bank(self, step, use):
        return self.index(step, use)[0] % 2

    def full(self, step, use):
        fixed, more = self.index(step, use)
        return more * len(self.order) + (fixed + 1)

    def freed(self, step, use):
        fixed, more = self.index(step, use)
        return more * (len(self.order) // 2) + fixed // 2

    def total(self):
        return self.before + NB * len(self.order)


RING_PM_A, RING_ST_A = Ring(PM_A), Ring(ST_A)
RING_PM_B, RING_ST_B = Ring(PM_B, RING_PM_A.total()), Ring(ST_B, RING_ST_A.total())


def consts():
    pos = np.arange(T, dtype=np.float32).reshape(NT, P)

    def freq(d, n):
        return (np.float32(1.0) / np.float32(10000.0) ** (np.arange(0, d, 2, dtype=np.float32) / np.float32(d)))

    fa = freq(DA, DA // 2)
    ang = pos[:, :, None] * fa[None, None, :]
    ca = np.concatenate([np.cos(ang), -np.cos(ang)], -1)
    sa = np.concatenate([np.sin(ang), np.sin(ang)], -1)
    fb = (np.float32(10000.0) ** (-np.arange(0, DB, 2, dtype=np.float32) / np.float32(DB))).astype(np.float32)
    ang = (pos[:, :, None] * fb[None, None, :]).astype(np.float32)
    cb = np.concatenate([np.cos(ang), np.cos(ang)], -1)
    sb = np.concatenate([-np.sin(ang), np.sin(ang)], -1)
    rot = np.concatenate([x.transpose(1, 0, 2).reshape(P, -1) for x in (ca, sa, cb, sb)], 1)
    p = np.arange(P)
    tri = (p[:, None] <= p[None, :]).astype(np.float32)
    iota = np.tile(np.arange(E, dtype=np.float32), (P, 1))
    f = np.concatenate([np.eye(P), rot, iota, E - iota, np.ones((P, P))], 1).astype(np.float32)
    add_row = np.eye(P)
    add_row[0] = 1.0
    by_query = np.where(p[None, :] > p[:, None], NEG, 0.0)
    by_key = by_query.T.copy()
    b = np.concatenate([np.eye(P), add_row, by_query, by_key, np.ones((P, P)), tri], 1)
    return f, b.astype(np.float32).astype(np.dtype("bfloat16"))


ROT = NT * DA * 2 + NT * DB * 2
CF_ID, CF_ROT, CF_IOTA, CF_DOWN, CF_ONES = 0, P, P + ROT, P + ROT + E, P + ROT + 2 * E
CF = CF_ONES + P
CB_ID, CB_ADD, CB_QMASK, CB_KMASK, CB_ONES, CB_TRI = (P * i for i in range(6))
CB = 6 * P
WB_IN = 16 * 8
CHAIN_A, CHAIN_B = 2 * NT + 4, 2 + 4
R96 = 3 * 4 * DA
HK = HID // P
GT = NG // P
NGROUPS = NB * T // NG
CHAIN_F = 2 * GT + 3 + 3 * 4
W_IN = 16 * 9


def build(nc, x, Wq, bq, Wk, bk, Wv, bv, Wo, bo, g1, g2, wq, wk, wv, wo, router_w, router_b,
          w1, w2, w3, cf, cb, out):
    with ExitStack() as ctx:
        inv_dram = nc.dram_tensor("inv_dram", (2 * H, P), F32, kind="Internal").ap()
        def sb(name, shape, dt=F32):
            return ctx.enter_context(nc.sbuf_tensor(name, shape, dt))

        def psum(name, shape):
            return ctx.enter_context(nc.psum_tensor(name, shape, F32))

        def sem(name):
            return ctx.enter_context(nc.semaphore(name))

        ps_st = psum("ps_st", [P, 2, 2, 512])
        ps_pm = psum("ps_pm", [P, 2, 512])
        ps_o = psum("ps_o", [P, 2, 512])

        cft = sb("cft", [P, CF])
        cbt = sb("cbt", [P, CB], BF16)
        ident = cft[:, CF_ID:CF_ID + P]
        ones_f = cft[:, CF_ONES:CF_ONES + P]
        rot_a = cft[:, CF_ROT:CF_ROT + 2 * NT * DA].rearrange("p (k t d) -> p k t d", k=2, t=NT)
        rot_b = cft[:, CF_ROT + 2 * NT * DA:CF_ROT + ROT].rearrange("p (k t d) -> p k t d", k=2, t=NT)
        tri = cbt[:, CB_TRI:CB_TRI + P]
        iota = cft[:, CF_IOTA:CF_IOTA + E]
        down = cft[:, CF_DOWN:CF_DOWN + E]
        ident_b = cbt[:, CB_ID:CB_ID + P]
        add_row = cbt[:, CB_ADD:CB_ADD + P]
        qmask = cbt[:, CB_QMASK:CB_QMASK + P]
        kmask = cbt[:, CB_KMASK:CB_KMASK + P]
        ones_b = cbt[0:1, CB_ONES:CB_ONES + P]
        wa_raw = sb("wa_raw", [P, C + 2 * DA])
        ba_raw = sb("ba_raw", [1, C + 2 * DA])
        wa = sb("wa", [P, QA + DA])
        ba = sb("ba", [1, QA + DA])
        woa = sb("woa", [P, C])
        boa = sb("boa", [1, C])
        wqkv = sb("wqkv", [P, (H + 2 * HKV) * DB])
        wob = sb("wob", [P, H * DB // P, C])
        g1b = sb("g1b", [P, C])
        g2b = sb("g2b", [P, C])
        rw = sb("rw", [P, E])
        rb = sb("rb", [1, E])

        x_all = sb("x_all", [P, NTILES, C])
        x1_all = sb("x1_all", [P, NTILES, C])
        z_all = x1_all
        xf_all = x_all
        xfT_all = sb("xfT_all", [P, NTILES * P])
        lg_all = sb("lg_all", [P, NTILES, E])

        xs = [sb(f"xs{u}", [P, NT, C]) for u in range(2)]
        xT = [sb(f"xT{u}", [P, T]) for u in range(2)]
        qbuf = [sb(f"qbuf{u}", [P, H * T], F32R) for u in range(2)]
        q96 = [b[0:R96, 0:4 * T].rearrange("p (b t) -> p b t", b=4) for b in qbuf]
        qhi = [b[:, 0:H // 2 * T].rearrange("p (j t) -> p j t", j=H // 2) for b in qbuf]
        qlo = [b[:, H // 2 * T:].rearrange("p (j t) -> p j t", j=H // 2) for b in qbuf]
        kbuf = [sb(f"kbuf{u}", [P, 4 * T + HKV // 2 * T], F32R) for u in range(2)]
        k96 = [b[0:R96, 0:4 * T].rearrange("p (a t) -> p a t", a=4) for b in kbuf]
        kdiag = [b[:, 0:4 * T].rearrange("p (j b t) -> p j b t", j=HKV // 2, b=2) for b in kbuf]
        klo = [b[:, 4 * T:].rearrange("p (j t) -> p j t", j=HKV // 2) for b in kbuf]
        pt = sb("pt", [P, 3, H, P])
        nrow = sb("nrow", [P, H, T], BF16)
        negmax = sb("negmax", [2 * H, P], BF16)
        rmax = sb("rmax", [P, NT * H])
        qkr = sb("qkr", [P, NT, QB + HKV * DB])
        prod = sb("prod", [P, 2, 512])
        qh = sb("qh", [P, T], F32R)
        ql = sb("ql", [P, T], F32R)
        khr = sb("khr", [P, NT, DA], F32R)
        kz = sb("kz", [P, NT, 4 * (R96 + DA)])
        va = [sb(f"va{u}", [P, NT, 4, 2, 4 * DA]) for u in range(2)]
        vb = [sb(f"vb{u}", [P, NT, HKV, 2 * DB]) for u in range(2)]
        pvb = [sb(f"pvb{u}", [P, 2, NT, HKV // 2, 512]) for u in range(2)]
        flat0, flat1 = (b[:, :, :, :, :].rearrange("p a b c d -> p (a b c d)") for b in pvb)
        pvs = flat0[0:8 * DA, 0:NT * 512].rearrange("p (t c) -> p t c", t=NT)
        ora, ords = flat0[:, 1024:1024 + T], flat0[:, 1280:1280 + T]
        w1s, w2s = (flat0[:, E * HID * i:E * HID * (i + 1)].rearrange("p (e n) -> p e n", e=E) for i in range(2))
        w3s = flat1[:, 0:E * HID // P * C].rearrange("p (e k c) -> p e k c", e=E, k=HID // P)
        w12h, w12l = (b[:, 0:2 * E * HID].rearrange("p (w e n) -> p w e n", w=2, e=E) for b in qbuf)
        xgh, xgl = (b[:, 0:NG] for b in kbuf)
        wh_in, wl_in = sem("wh_in"), sem("wl_in")
        xgh_in, xgl_in = sem("xgh_in"), sem("xgl_in")
        sums = sb("sums", [2 * H, P])
        oT = sb("oT", [P, NT, HKV // 2, G, P])
        y = sb("y", [P, NT, C])
        stat = sb("stat", [P, NT, 6])
        mv = sb("mv", [P, NT, 2])
        junk = sb("junk", [P, NT, C])
        xn = sb("xn", [P, NT, C])
        xf = sb("xf", [P, NT, C])
        xfT = sb("xfT", [P, T])

        class Root:
            def __init__(self, name):
                self.ss, self.v, self.ln, self.r0, self.a, self.r = (
                    sb(f"{name}_{x}", [P, NT]) for x in ("ss", "v", "ln", "r0", "a", "r"))
        root_p, root_t = Root("root_p"), Root("root_t")

        top = sb("top", [P, 2, NTILES])
        oh = sb("oh", [P, 2, NTILES, E])
        oh_b = sb("oh_b", [P, 2, NTILES, E], BF16)
        rt = sb("rt", [P, 2, NTILES, E])
        ru = sb("ru", [P, 4, NTILES])
        score = sb("score", [P, 2, NTILES])
        fits = sb("fits", [P, 2, NTILES])
        wx = sb("wx", [P, NTILES])
        we = sb("we", [P, NTILES, E])
        weg = sb("weg", [P, GT, E])
        asb = prod
        gated = pt[:, 0].rearrange("p h t -> p (h t)")[:, 0:1024].rearrange("p (a b) -> p a b", a=2)
        hid = pt[:, 1].rearrange("p h t -> p (h t)")[:, 0:2048].rearrange("p (a k b) -> p a k b", a=2, k=HK)
        carrier = sb("carrier", [P, 1])
        fstat = sb("fstat", [P, GT, 6])
        fmv = sb("fmv", [P, GT, 2])
        froot = sb("froot", [P, 3, GT])
        oh_in, e_in, cnt_in, chain_r = sem("oh_in"), sem("e_in"), sem("cnt_in"), sem("chain_r")
        up_full = sem("up_full")
        a_in = sem("a_in")
        prod_e = sem("prod_e")
        hid_in = sem("hid_in")
        down_full = sem("down_full")
        acc0_in, acc_in = sem("acc0_in"), sem("acc_in")
        chain_f, fin_in = sem("chain_f"), sem("fin_in")
        inv_sb = sem("inv_sb")
        oTa = oT[:, 0, 0, 0:2, :].rearrange("p g c -> p (g c)")

        def groups(eng, body):
            body(0)
            with eng.Fori(1, NGROUPS - 1) as j:
                body(j)
            body(NGROUPS - 1)

        def another(j):
            return not isinstance(j, int) or j + 1 < NGROUPS

        w_in = sem("w_in")
        wb_in = sem("wb_in")
        w12_in, w3_in = sem("w12_in"), sem("w3_in")
        wo_in = sem("wo_in")
        x0_in, x_in = sem("x0_in"), sem("x_in")
        prep = sem("prep")
        zeroed = sem("zeroed")
        pm_full, st_full = sem("pm_full"), sem("st_full")
        pm_free = [sem("pm_free0"), sem("pm_free1")]
        st_free = [sem("st_free0"), sem("st_free1")]
        sc_full = sem("sc_full")
        probs = sem("probs")
        xs_in = sem("xs_in")
        xn_in = sem("xn_in")
        prod_in = sem("prod_in")
        rot_in = sem("rot_in")
        add_in = sem("add_in")
        va_in = sem("va_in")
        v_in = sem("v_in")
        hi_in = sem("hi_in")
        kz_in = sem("kz_in")
        chain_k = sem("chain_k")
        q_dma = sem("q_dma")
        n_dma = sem("n_dma")
        o_dma = sem("o_dma")
        s_dma = sem("s_dma")
        i_dma = sem("i_dma")
        b_dma = sem("b_dma")
        inv_in = sem("inv_in")
        oT_in = sem("oT_in")
        chain_p, chain_t = sem("chain_p"), sem("chain_t")
        var_p, var_t = sem("var_p"), sem("var_t")
        ln_p, ln_t = sem("ln_p"), sem("ln_t")
        r0_p, r0_t = sem("r0_p"), sem("r0_t")
        x1_in = sem("x1_in")
        z_in = sem("z_in")
        xf_in = sem("xf_in")
        xfa_in = sem("xfa_in")
        out_dma = sem("out_dma")

        def tiles(ap, n):
            return ap[:, bass.ds(n * NT, NT), :]

        def emptied(eng, ring, step, use):
            free = pm_free if ring in (RING_PM_A, RING_PM_B) else st_free
            eng.wait_ge(free[ring.bank(step, use)], ring.freed(step, use) + 1)

        def some(value):
            return not isinstance(value, int) or value > 0

        def draining(s):
            return isinstance(s, int) and s >= NB - 1

        def pipeline(eng, step):
            def one(s, u):
                step(s, u, {x for x, a in AHEAD.items() if not isinstance(s, int) or 0 <= s + a < NB})

            for s in range(-2, FULL):
                one(s, s % 2)
            with eng.Fori(0, (NB - 2 - FULL) // 2) as j:
                one(2 * j + FULL, FULL % 2)
                one(2 * j + (FULL + 1), 1 - FULL % 2)
            for s in range(FULL + 2 * ((NB - 2 - FULL) // 2), NB + 1):
                one(s, s % 2)

        block = ctx.enter_context(nc.Block())

        @block.sync
        def _(sp):
            nc.sync.dma_start(cft[:, :], cf).then_inc(w_in, 16)
            nc.sync.dma_start(wa_raw[:, 0:C], Wq).then_inc(w_in, 16)
            nc.sync.dma_start(wa_raw[:, C:C + DA], Wk).then_inc(w_in, 16)
            nc.sync.dma_start(wa_raw[:, C + DA:], Wv).then_inc(w_in, 16)
            nc.sync.dma_start(cbt[:, :], cb).then_inc(w_in, 16)
            for i, b in enumerate((bq, bk, bv)):
                lo = [0, C, C + DA][i]
                nc.sync.dma_start(ba_raw[:, lo:lo + b.shape[0]], b[None, :]).then_inc(w_in, 16)
            nc.sync.dma_start(boa[:, :], bo[None, :]).then_inc(w_in, 16)

            def row_of_max(ring, s):
                emptied(sp, ring, s, "nmT")
                for t in range(NT):
                    nc.sync.dma_start(nrow[0:1, :, P * t:P * (t + 1)],
                                      negmax[H * t:H * (t + 1), :]).then_inc(n_dma, 16)

            def step_a(s, u, on):
                if "M" in on:
                    row_of_max(RING_PM_A, s)
                if "P" in on:
                    emptied(sp, RING_PM_A, s, "qT")
                    for i, part in enumerate((qh, qh, ql)):
                        nc.sync.dma_start(q96[u][4 * DA * i:4 * DA * (i + 1), :, :].bitcast(F32),
                                          part[:, :].bitcast(F32)).then_inc(q_dma, 16)
                if "S" in on:
                    emptied(sp, RING_ST_A, s, "pv1")
                    for t in range(NT):
                        for to, lo in ((ora, 0), (ords, 4 * DA)):
                            nc.sync.dma_start(to[:, P * t:P * (t + 1)], pvs[lo:lo + 4 * DA, t, :]) \
                                .then_inc(o_dma, 16)

            for q in range(4):
                rows = 4 * DA
                nc.sync.dma_start(woa[rows * q:rows * (q + 1), :],
                                  Wo[rows * q:rows * (q + 1), :].rearrange("(h d) c -> d h c", d=DA)) \
                    .then_inc(wo_in, 16)
            pipeline(sp, step_a)

            def step_b(s, u, on):
                if "T" in on:
                    sp.wait_ge(inv_sb, s)
                    nc.sync.dma_start(inv_dram, sums[:, :]).then_inc(i_dma, 16)
                    sp.wait_ge(i_dma, 16 * s)
                    for b in range(2):
                        nc.sync.dma_start(oT[DB * b:DB * (b + 1)].rearrange("p t k g c -> p (t k g c)"),
                                          inv_dram[H * b:H * (b + 1), :].rearrange("(o h) c -> o (h c)", o=1)
                                          .broadcast_to([DB, H * P])) \
                            .then_inc(b_dma, 16)
                if "M" in on:
                    row_of_max(RING_PM_B, s)
                if "S" in on:
                    emptied(sp, RING_ST_B, s, "pv7")
                    for b in range(2):
                        lone = DB * (1 - b)
                        nc.sync.dma_start(sums[H * b:H * (b + 1), :],
                                          pvb[u][lone:lone + 1, b].rearrange("o t j c -> o (t j c)")) \
                            .then_inc(s_dma, 16)

            pipeline(sp, step_b)

            sp.wait_ge(oT_in, NB + NB - 1)
            nc.sync.dma_start(w1s, w1.rearrange("e c h -> c e h")).then_inc(w12_in, 16)
            nc.sync.dma_start(w2s, w2.rearrange("e c h -> c e h")).then_inc(w12_in, 16)
            sp.wait_ge(oT_in, NB + NB)
            nc.sync.dma_start(w3s, w3.rearrange("e (k p) c -> p e k c", p=P)).then_inc(w3_in, 16)

            def store(j):
                sp.wait_ge(fin_in, j + 1)
                nc.sync.dma_start(out.rearrange("b (t p) c -> p (b t) c", p=P)[:, bass.ds(j * GT, GT), :],
                                  z_all[:, bass.ds(j * GT, GT), :]).then_inc(out_dma, 16)
            groups(sp, store)
            sp.wait_ge(out_dma, 16 * NGROUPS)

        @block.gpsimd
        def _(pool):
            nc.gpsimd.memset(kz[:, :, :], 0.0).then_inc(zeroed, 1)
            for u in range(2):
                nc.gpsimd.memset(va[u][:, :, :, :, :], 0.0).then_inc(zeroed, 1)
            pool.wait_ge(zeroed, 3)
            for u in range(2):
                for q in range(4):
                    nc.gpsimd.memset(va[u][:, :, q, 1, DA * q:DA * (q + 1)], 1.0)
                nc.gpsimd.memset(vb[u][:, :, :, :], 1.0).then_inc(prep, 1)
            pool.wait_ge(w_in, W_IN)
            nc.gpsimd.tensor_copy(nrow[:, :, :].rearrange("p h (t c) -> p (h t) c", t=NT),
                                  kmask.unsqueeze(1).broadcast_to([P, H * NT, P])).then_inc(prep, 1)

            def step_a(s, u, on):
                if "P" in on:
                    n = s + 2
                    if some(n - 1):
                        pool.wait_ge(rot_in, n - 1)
                    pool.wait_ge(*(x0_in, 16) if isinstance(n, int) and n == 0 else (x_in, 16))
                    nc.gpsimd.tensor_copy(xs[u][:, :, :], tiles(x_all, n)).then_inc(xs_in, 1)

            pipeline(pool, step_a)

            def step_b(s, u, on):
                n, m = s + 2, s - 1
                if "P" in on:
                    if some(n - 1):
                        pool.wait_ge(xn_in, n - 1)
                    nc.gpsimd.tensor_copy(xs[u][:, :, :], tiles(x1_all, n)).then_inc(xs_in, 1)
                if "T" in on and not draining(s):
                    pool.wait_ge(b_dma, 32 * s)
                    for b in range(2):
                        if "P" in on:
                            pool.wait_ge(xs_in, NB + n + 1)
                        else:
                            pool.wait_ge(v_in, NB)
                            pool.wait_ge(xfa_in, m)
                        for t in range(NT):
                            half = slice(DB * b, DB * (b + 1))
                            ins = nc.gpsimd.tensor_tensor(
                                oT[half, t], pvb[1 - u][half, b, t, :, :].rearrange("p k (g c) -> p k g c", g=G),
                                oT[half, t], ALU.mult)
                    ins.then_inc(oT_in, 1)
                    pool.wait_ge(oT_in, NB + s)

                def add_rotary(t):
                    for i in range(3):
                        emptied(pool, RING_PM_B, s, f"qkv{t}{i}")
                        w = 512 if i < 2 else HKV * DB
                        part = qkr[:, t, 512 * i:512 * i + w]
                        nc.gpsimd.tensor_tensor(part, part, prod[:, (3 * t + i) % 2, 0:w], ALU.add) \
                            .then_inc(add_in, 1)

                if "P" in on:
                    add_rotary(0)
                    add_rotary(1)
                if "P" in on:
                    pool.wait_ge(pm_full, RING_PM_B.full(s, "qkT00"))
                if "T" in on:
                    pool.wait_ge(xf_in, m + 1)
                    nc.gpsimd.tensor_copy(tiles(xf_all, m), xf[:, :, :])
                    emptied(pool, RING_ST_B, s, "xfT")
                    nc.gpsimd.tensor_copy(xfT_all[:, bass.ds(m * T, T)], xfT[:, :]).then_inc(xfa_in, 1)
                if "P" in on:
                    for b in range(2):
                        for t in range(NT):
                            v = qkr[:, t, QB:].rearrange("p (k b d) -> p k b d", b=2, d=DB)[:, :, b, :]
                            ins = nc.gpsimd.tensor_copy(vb[u][:, t, b::2, DB * b:DB * (b + 1)], v)
                    ins.then_inc(v_in, 1)

            pool.wait_ge(x1_in, NB)
            for u in range(2):
                nc.gpsimd.memset(kdiag[u][:, :, :, :].bitcast(F32), 0.0).then_inc(zeroed, 1)
            pipeline(pool, step_b)

            for e in range(0, E, 2):
                for w in range(2):
                    pool.wait_ge(wh_in, e + (w + 1))
                    nc.gpsimd.tensor_tensor(w12l[:, w, e:e + 2, :], (w1s, w2s)[w][:, e:e + 2, :],
                                            w12h[:, w, e:e + 2, :].bitcast(F32), ALU.subtract).then_inc(wl_in, 1)

        @block.tensor
        def _(pe):
            def pm(ring, s, use):
                b, f = ring.bank(s, use), ring.freed(s, use)
                if some(f):
                    pe.wait_ge(pm_free[b], f)
                return ps_pm[:, b, :]

            def st(ring, s, use):
                b, f = ring.bank(s, use), ring.freed(s, use)
                if some(f):
                    pe.wait_ge(st_free[b], f)
                return ps_o[:, b, :]

            def mask_rows(ring, s, i):
                o = pm(ring, s, f"m{i}")
                heads = 4 if i < 4 else 2
                o = o.rearrange("p (h k) -> p h k", h=heads)
                nc.tensor.matmul(o[:, :, P * (i >= 4):], ident_b, qmask.unsqueeze(1).broadcast_to([P, heads, P]),
                                 start=True, stop=False, skip_group_check=True)
                return o

            def max_rows(ring, s):
                o = pm(ring, s, "nmT")
                emptied(pe, ring, s, "m11")
                nc.tensor.transpose(o[0:NT * H, 0:P], rmax[:, :], ident).then_inc(pm_full, 1)

            def key_scores(count, c, products):
                kind, half = CHUNKS[c]
                kt, qt = BLOCKS[kind]
                need = count * NCH + (c - 1)
                if some(need):
                    pe.wait_ge(probs, need)
                for b in range(2):
                    o = ps_st[:, c % 2, b, :].rearrange("p (h t) -> p h t", h=4)
                    hs = slice(8 * half + 4 * b, 8 * half + 4 * b + 4)
                    for i, (k, q) in enumerate(products(hs, kt, qt)):
                        nc.tensor.matmul(o, k, q, start=i == 0, stop=False)
                    row = nrow[:, hs, P * qt:P * (qt + 1)]
                    if kind == OFF:
                        mm = nc.tensor.matmul(o, ones_b, row[0:1], start=False, stop=True)
                    else:
                        mm = nc.tensor.matmul(o, add_row, row, start=False, stop=True)
                mm.then_inc(sc_full, 1)

            def turn_x(ring, s, src):
                o = pm(ring, s, "xT")
                for t in range(NT):
                    mm = nc.tensor.transpose(o[:, P * t:P * (t + 1)], src[:, t, :], ident)
                mm.then_inc(pm_full, 1)

            pe.wait_ge(prep, 5)
            pe.wait_ge(w_in, W_IN)

            def step_a(s, u, on):
                n = s + 2

                def project_out():
                    if "T" in on:
                        for t in range(NT):
                            o = st(RING_ST_A, s, f"wo{t}")
                            if t == 0:
                                pe.wait_ge(oT_in, s)
                            pe.wait_ge(wo_in, 64)
                            nc.tensor.matmul(o[:, 0:C], oTa[:, P * t:P * (t + 1)], woa[:, :],
                                             start=True, stop=False)
                            nc.tensor.matmul(o[:, 0:C], ones_f[0:1], boa[:, :],
                                             start=False, stop=True).then_inc(st_full, 1)

                def scores(c):
                    if "S" in on:
                        key_scores(s, c, lambda hs, kt, qt: [(k96[u][:, hs.start // 4, P * kt:P * (kt + 1)],
                                                              q96[u][:, :, P * qt:P * (qt + 1)])])

                def values(qt):
                    if "S" in on:
                        o = st(RING_ST_A, s, f"pv{qt}")[0:8 * DA, :].rearrange("p (h t) -> p h t", h=4)
                        pe.wait_ge(probs, s * NCH + (2 if qt == 0 else NCH))
                        blocks = [(DIAG0, 0)] if qt == 0 else [(OFF, 0), (DIAG1, 1)]
                        for i, (kind, kt) in enumerate(blocks):
                            for q in range(4):
                                mm = nc.tensor.matmul(o, va[u][:, kt, q, :, :].rearrange("p k c -> p (k c)"),
                                                      pt[:, kind, 4 * q:4 * q + 4, :], start=i + q == 0,
                                                      stop=i == len(blocks) - 1 and q == 3)
                        mm.then_inc(st_full, 1)

                def project():
                    if "P" in on:
                        o = pm(RING_PM_A, s, "qkv")
                        emptied(pe, RING_PM_A, s, "xT")
                        k = QA + DA
                        for t in range(NT):
                            nc.tensor.matmul(o[:, k * t:k * (t + 1)], xT[u][:, P * t:P * (t + 1)], wa[:, :],
                                             start=True, stop=False)
                            mm = nc.tensor.matmul(o[:, k * t:k * (t + 1)], ones_f[0:1], ba[:, :],
                                                  start=False, stop=True)
                        mm.then_inc(pm_full, 1)

                def turn_qk():
                    if "P" in on:
                        o = pm(RING_PM_A, s, "qT")
                        pe.wait_ge(rot_in, n + 1)
                        for t in range(NT):
                            mm = nc.tensor.transpose(o[:, P * t:P * (t + 1)], qkr[:, t, 0:C], ident)
                        mm.then_inc(pm_full, 1)
                        pe.wait_ge(kz_in, n + 1)
                        for i in range(2):
                            o = pm(RING_PM_A, s, f"kT{i}")
                            for h in range(2):
                                for t in range(NT):
                                    lo = R96 * (2 * i + h)
                                    mm = nc.tensor.transpose(o[0:R96, T * h + P * t:T * h + P * (t + 1)],
                                                             kz[:, t, lo:lo + R96], ident)
                            mm.then_inc(pm_full, 1)

                def maxima(lo, hi):
                    if "M" in on:
                        if lo == 0:
                            pe.wait_ge(q_dma, 48 * (s + 2))
                            if "P" not in on:
                                emptied(pe, RING_PM_A, s - 1, "kT1")
                        for i in range(lo, hi):
                            o = mask_rows(RING_PM_A, s, i)
                            q, k = (q96[1 - u][:, i, 0:P], k96[1 - u][:, :, 0:P]) if i < 4 else \
                                (q96[1 - u][:, (i - 4) // 2, P:], k96[1 - u][:, 2 * (i % 2):2 * (i % 2) + 2, :])
                            nc.tensor.matmul(o, q, k, start=False, stop=True, skip_group_check=True) \
                                .then_inc(pm_full, 1)

                if "P" in on:
                    pe.wait_ge(xs_in, n + 1)
                    turn_x(RING_PM_A, s, xs[u])
                if "S" in on:
                    pe.wait_ge(n_dma, 32 * (s + 1))
                scores(0)
                maxima(0, 2)
                scores(1)
                maxima(2, 4)
                if "S" in on:
                    pe.wait_ge(va_in, s + 1)
                values(0)
                scores(2)
                maxima(4, 6)
                project()
                scores(3)
                maxima(6, 8)
                project_out()
                maxima(8, 10)
                scores(4)
                maxima(10, 12)
                scores(5)
                if "M" in on:
                    max_rows(RING_PM_A, s)
                turn_qk()
                values(1)

            pipeline(pe, step_a)

            def step_b(s, u, on):
                n = s + 2

                def scores(c):
                    def products(hs, kt, qt):
                        hk = hs.start // G
                        half, pair = slice(DB * (hk % 2), DB * (hk % 2 + 1)), hk // 2
                        kk, qq = slice(P * kt, P * (kt + 1)), slice(P * qt, P * (qt + 1))
                        kh, kl = kdiag[u][half, pair, hk % 2, kk], klo[u][half, pair, kk]
                        qh, ql = qhi[u][half, pair::2, qq], qlo[u][half, pair::2, qq]
                        return [(kh, qh), (kl, qh), (kh, ql)]
                    if "S" in on:
                        key_scores(s + NB, c, products)

                def maxima(lo, hi):
                    if "M" in on:
                        for i in range(lo, hi):
                            o = mask_rows(RING_PM_B, s, i)
                            if i < 4:
                                for j in range(2):
                                    mm = nc.tensor.matmul(o[:, 2 * j:2 * j + 2, :], qhi[1 - u][:, 2 * i + j, 0:P],
                                                          kdiag[1 - u][:, j, :, 0:P], start=False, stop=j == 1,
                                                          skip_group_check=True)
                            else:
                                mm = nc.tensor.matmul(o, qhi[1 - u][:, i - 4, P:], kdiag[1 - u][:, i % 2, :, :],
                                                      start=False, stop=True, skip_group_check=True)
                            mm.then_inc(pm_full, 1)

                def values(lo, hi):
                    for i in range(lo, hi) if "S" in on else ():
                        qt, hk = i // HKV, i % HKV
                        o = st(RING_ST_B, s, f"pv{i}")
                        pe.wait_ge(probs, (s + NB) * NCH + (1, 2, 4, NCH)[2 * qt + hk // 2])
                        blocks = [(DIAG0, 0)] if qt == 0 else [(OFF, 0), (DIAG1, 1)]
                        for j, (kind, kt) in enumerate(blocks):
                            mm = nc.tensor.matmul(o.rearrange("p (h t) -> p h t", h=G), vb[u][:, kt, hk, :],
                                                  pt[:, kind, G * hk:G * (hk + 1), :], start=j == 0,
                                                  stop=j == len(blocks) - 1)
                        mm.then_inc(st_full, 1)

                def project(t):
                    if "P" in on:
                        if t == 0:
                            emptied(pe, RING_PM_B, s, "xT")
                        for i in range(3):
                            o = pm(RING_PM_B, s, f"qkv{t}{i}")
                            nc.tensor.matmul(o, xT[u][:, P * t:P * (t + 1)], wqkv[:, 512 * i:512 * (i + 1)],
                                             start=True, stop=True).then_inc(pm_full, 1)

                def turn_qk(t):
                    for i in range(3) if "P" in on else ():
                        o = pm(RING_PM_B, s, f"qkT{t}{i}")
                        pe.wait_ge(add_in, 6 * n + (3 * t + i + 1))
                        for j in range(4 if i < 2 else 2):
                            mm = nc.tensor.transpose(o[:, P * j:P * (j + 1)],
                                                     qkr[:, t, 512 * i + P * j:512 * i + P * (j + 1)], ident)
                        mm.then_inc(pm_full, 1)

                def project_out():
                    for t in range(NT) if "T" in on else ():
                        o = st(RING_ST_B, s, f"wo{t}")
                        if t == 0:
                            pe.wait_ge(oT_in, NB + s)
                        for j in range(H // 2):
                            mm = nc.tensor.matmul(o[:, 0:C], oT[:, t, j % 2, j // 2, :], wob[:, j, :],
                                                  start=j == 0, stop=j == H // 2 - 1)
                        mm.then_inc(st_full, 1)

                if "S" in on:
                    pe.wait_ge(n_dma, 32 * (NB + s + 1))
                scores(0)
                maxima(0, 2)
                scores(1)
                maxima(2, 4)
                if "S" in on:
                    pe.wait_ge(v_in, s + 1)
                values(0, 2)
                if "P" in on:
                    pe.wait_ge(xn_in, n + 1)
                    turn_x(RING_PM_B, s, xn)
                scores(2)
                maxima(4, 6)
                values(2, 4)
                scores(3)
                maxima(6, 8)
                project(0)
                values(4, 6)
                maxima(8, 10)
                scores(4)
                project_out()
                project(1)
                maxima(10, 12)
                scores(5)
                if "M" in on:
                    max_rows(RING_PM_B, s)
                values(6, 8)
                if "T" in on:
                    o = st(RING_ST_B, s, "xfT")
                    pe.wait_ge(xf_in, s)
                    for t in range(NT):
                        mm = nc.tensor.transpose(o[:, P * t:P * (t + 1)], xf[:, t, :], ident)
                    mm.then_inc(st_full, 1)
                turn_qk(0)
                if "T" in on:
                    o = st(RING_ST_B, s, "lg")
                    emptied(pe, RING_ST_B, s, "xfT")
                    for t in range(NT):
                        nc.tensor.matmul(o[:, E * t:E * (t + 1)], xfT[:, P * t:P * (t + 1)], rw[:, :],
                                         start=True, stop=False)
                        mm = nc.tensor.matmul(o[:, E * t:E * (t + 1)], ones_f[0:1], rb[:, :],
                                              start=False, stop=True)
                    mm.then_inc(st_full, 1)
                turn_qk(1)

            pe.wait_ge(wb_in, WB_IN)
            pipeline(pe, step_b)

            def counts():
                pe.wait_ge(oh_in, 1)
                o = ps_o[:, 0, 0:2 * NTILES * E].rearrange("p (k t e) -> p k t e", k=2, t=NTILES)
                nc.tensor.matmul(o, tri, oh_b[:, :, :, :], start=True, stop=False, skip_group_check=True)
                for i in range(NTILES - 1):
                    mm = nc.tensor.matmul(o[:, :, i + 1:, :], cbt[:, CB_ONES:CB_ONES + P],
                                          oh_b[:, :, i, :].unsqueeze(2).broadcast_to([P, 2, NTILES - 1 - i, E]),
                                          start=False, stop=i == NTILES - 2, skip_group_check=True)
                mm.then_inc(cnt_in, 1)

            def group(j):
                pe.wait_ge(xgl_in, j + 1)

                def up(e):
                    for k in range(HK):
                        i = HK * e + k
                        need = j * (E * HK) + (i - 1)
                        if some(need):
                            pe.wait_ge(prod_e, need)
                        for w in range(2):
                            pe.wait_ge(wl_in, 2 * (e // 2) + (w + 1))
                            wh, wl = w12h[:, w, e, P * k:P * (k + 1)], w12l[:, w, e, P * k:P * (k + 1)]
                            nc.tensor.matmul(ps_st[:, i % 2, w, :], wh, xgh, start=True, stop=False)
                            nc.tensor.matmul(ps_st[:, i % 2, w, :], wh, xgl, start=False, stop=False)
                            mm = nc.tensor.matmul(ps_st[:, i % 2, w, :], wl, xgh, start=False, stop=True)
                        mm.then_inc(up_full, 1)

                def down(e):
                    pe.wait_ge(hid_in, j * (E * HK) + HK * (e + 1))
                    need = j * E + (e - 1)
                    if some(need):
                        pe.wait_ge(acc_in, need)
                    for t in range(GT):
                        for k in range(HK):
                            mm = nc.tensor.matmul(ps_pm[:, e % 2, C * t:C * (t + 1)], hid[:, e % 2, k, P * t:P * (t + 1)],
                                                  w3s[:, e, k, :], start=k == 0, stop=k == HK - 1)
                    mm.then_inc(down_full, 1)

                up(0)
                for e in range(E):
                    if e + 1 < E:
                        up(e + 1)
                    down(e)

            pe.wait_ge(xfa_in, NB)
            counts()
            pe.wait_ge(w3_in, 16)
            groups(pe, group)

        @block.vector
        def _(dve):
            def newton(root, chain, at):
                nc.vector.tensor_tensor(root.a[:, :], root.r0[:, :], root.r0[:, :], ALU.mult).then_inc(chain, 1)
                dve.wait_ge(chain, at + 1)
                nc.vector.tensor_tensor(root.a[:, :], root.a[:, :], root.v[:, :], ALU.mult).then_inc(chain, 1)
                dve.wait_ge(chain, at + 2)
                nc.vector.tensor_scalar(root.a[:, :], root.a[:, :], -0.5, 1.5, ALU.mult, ALU.add).then_inc(chain, 1)
                dve.wait_ge(chain, at + 3)
                nc.vector.tensor_tensor(root.r[:, :], root.r0[:, :], root.a[:, :], ALU.mult).then_inc(chain, 1)
                dve.wait_ge(chain, at + 4)

            def mean_square(src, root, chain, at, var):
                for t in range(NT):
                    nc.vector.tensor_tensor_reduce(junk[:, t, :], src[:, t, :], src[:, t, :], 1.0, 0.0, ALU.mult,
                                                   ALU.add, root.ss[:, t:t + 1]).then_inc(chain, 1)
                dve.wait_ge(chain, at + 2)
                nc.vector.tensor_scalar(root.v[:, :], root.ss[:, :], 1.0 / C, EPS_RMS, ALU.mult, ALU.add) \
                    .then_inc(var, 1)

            dve.wait_ge(w_in, W_IN)
            for raw, to in ((wa_raw, wa), (ba_raw, ba)):
                nc.vector.tensor_copy(to[:, 0:C].rearrange("p (a d b) -> p a d b", a=4, d=DA),
                                      raw[:, 0:C].rearrange("p (a b d) -> p a d b", a=4, d=DA))
                nc.vector.tensor_copy(to[:, C:], raw[:, C:]).then_inc(prep, 1)

            def reduce_rows(ring, s, lo, hi, heads_of):
                for i in range(lo, hi):
                    b = ring.bank(s, f"m{i}")
                    dve.wait_ge(pm_full, ring.full(s, f"m{i}"))
                    nc.vector.tensor_reduce(heads_of(i), ps_pm[:, b, :].rearrange("p (h k) -> p h k", h=4 if i < 4 else 2),
                                            AX.X, ALU.max).then_inc(pm_free[b], 1)

            def step_a(s, u, on):
                n, m = s + 2, s - 1

                def heads(i):
                    r = rmax.rearrange("p (t a b) -> p t a b", t=NT, a=4)
                    return r[:, 0, :, i] if i < 4 else r[:, 1, 2 * (i % 2):2 * (i % 2) + 2, (i - 4) // 2]

                def maxima(lo, hi):
                    if "M" in on:
                        reduce_rows(RING_PM_A, s, lo, hi, heads)

                def rotate():
                    if "P" not in on:
                        return
                    b = RING_PM_A.bank(s, "qkv")
                    dve.wait_ge(pm_full, RING_PM_A.full(s, "qkv"))
                    src = ps_pm[:, b, 0:NT * (QA + DA)].rearrange("p (t k) -> p t k", t=NT)
                    m1, m2 = (prod[:, i, 0:NT * QA].rearrange("p (t k) -> p t k", t=NT) for i in range(2))
                    half = DA // 2
                    for lo, hi, of, k, m in ((0, DA, 0, 0, m1), (0, half, half, 1, m2), (half, DA, 0, 1, m2)):
                        for t in range(NT):
                            def cols(ap, at):
                                return ap[:, t, 0:C].rearrange("p (a d b) -> p a d b", a=4, d=DA)[:, :, at:at + hi - lo, :]
                            tab = rot_a[:, k, t, lo:hi].unsqueeze(1).unsqueeze(3).broadcast_to([P, 4, hi - lo, 4])
                            nc.vector.tensor_tensor(cols(m, lo), cols(src, of), tab, ALU.mult)
                        nc.vector.tensor_tensor(m[:, :, C + lo:C + hi], src[:, :, C + of:C + of + hi - lo],
                                                rot_a[:, k, :, lo:hi], ALU.mult).then_inc(prod_in, 1)
                    nc.vector.tensor_copy(qkr[:, :, QA:QA + DA], src[:, :, QA:]).then_inc(pm_free[b], 1)
                    dve.wait_ge(prod_in, 3 * (n + 1))
                    nc.vector.tensor_tensor(qkr[:, :, 0:QA], m1, m2, ALU.add).then_inc(rot_in, 1)
                    dve.wait_ge(rot_in, n + 1)
                    nc.vector.tensor_copy(khr[:, :, :], qkr[:, :, C:QA]).then_inc(chain_k, 1)
                    dve.wait_ge(chain_k, n + 1)
                    hi_k = khr[:, :, :].bitcast(F32).unsqueeze(2).broadcast_to([P, NT, 4, DA])
                    all_k = qkr[:, :, C:QA].unsqueeze(2).broadcast_to([P, NT, 4, DA])
                    places = kz[:, :, :].rearrange("p t (a r) -> p t a r", a=4)
                    for i in range(3):
                        to = places[:, :, :, 4 * DA * i:4 * DA * i + DA]
                        if i == 1:
                            nc.vector.tensor_tensor(to, all_k, hi_k, ALU.subtract)
                        else:
                            ins = nc.vector.tensor_copy(to, hi_k)
                    ins.then_inc(kz_in, 1)

                def split():
                    if "P" not in on:
                        return
                    b = RING_PM_A.bank(s, "qT")
                    dve.wait_ge(hi_in, n + 1)
                    nc.vector.tensor_tensor(ql[:, :], ps_pm[:, b, 0:T], qh[:, :].bitcast(F32), ALU.subtract) \
                        .then_inc(pm_free[b], 1)
                    if "S" in on:
                        dve.wait_ge(st_full, RING_ST_A.full(s, "pv1"))
                    for q in range(4):
                        ins = nc.vector.tensor_copy(va[u][:, :, q, 0, DA * q:DA * (q + 1)], qkr[:, :, QA:QA + DA])
                    ins.then_inc(va_in, 1)

                def normalise():
                    if "T" not in on:
                        return
                    dve.wait_ge(o_dma, 64 * s)
                    nc.vector.reciprocal(ords[:, :], ords[:, :]).then_inc(inv_in, 1)
                    dve.wait_ge(inv_in, s)
                    nc.vector.tensor_tensor(oTa, ora[:, :], ords[:, :], ALU.mult).then_inc(oT_in, 1)

                def residual():
                    if "T" not in on:
                        return
                    dve.wait_ge(x0_in, 16)
                    dve.wait_ge(x_in, 16)
                    for t in range(NT):
                        b = RING_ST_A.bank(s, f"wo{t}")
                        dve.wait_ge(st_full, RING_ST_A.full(s, f"wo{t}"))
                        nc.vector.tensor_tensor(y[:, t, :], ps_o[:, b, 0:C], tiles(x_all, m)[:, t, :],
                                                ALU.add).then_inc(st_free[b], 1)
                    for t in range(NT):
                        emptied(dve, RING_ST_A, s, f"wo{t}")
                        nc.vector.bn_stats(stat[:, t, :], y[:, t, :]).then_inc(chain_t, 1)
                    dve.wait_ge(chain_t, CHAIN_A * m + NT)
                    nc.vector.memset(carrier[:, :], 0.0)
                    for t in range(NT):
                        nc.vector.bn_aggr(mv[:, t, :], stat[:, t, :]).then_inc(chain_t, 1)
                    dve.wait_ge(chain_t, CHAIN_A * m + 2 * NT)
                    nc.vector.tensor_scalar(root_t.v[:, :], mv[:, :, 1], EPS_LN, None, ALU.add).then_inc(var_t, 1)

                def layernorm():
                    if "T" not in on:
                        return
                    dve.wait_ge(r0_t, m + 1)
                    newton(root_t, chain_t, CHAIN_A * m + 2 * NT)
                    for t in range(NT):
                        ins = nc.vector.tensor_scalar(tiles(x1_all, m)[:, t, :], y[:, t, :], mv[:, t, 0:1],
                                                      root_t.r[:, t:t + 1], ALU.subtract, ALU.mult)
                    ins.then_inc(x1_in, 1)

                maxima(0, 4)
                normalise()
                maxima(4, 6)
                rotate()
                maxima(6, 8)
                residual()
                maxima(8, 12)
                layernorm()
                split()

            pipeline(dve, step_a)

            def step_b(s, u, on):
                n, m = s + 2, s - 1

                def heads(i):
                    r = rmax.rearrange("p (t k g) -> p t k g", t=NT, k=HKV)
                    return r[:, 0, :, i] if i < 4 else r[:, 1, 2 * (i % 2):2 * (i % 2) + 2, (i - 4) // 2]

                def maxima(lo, hi):
                    if "M" in on:
                        reduce_rows(RING_PM_B, s, lo, hi, heads)

                def rotate(t):
                    for i in range(3) if "P" in on else ():
                        b = RING_PM_B.bank(s, f"qkv{t}{i}")
                        dve.wait_ge(pm_full, RING_PM_B.full(s, f"qkv{t}{i}"))
                        at = 6 * n + (3 * t + i)
                        if some(at - 1):
                            dve.wait_ge(add_in, at - 1)
                        w, nh = (512, 8) if i < 2 else (HKV * DB, HKV)
                        half = DB // 2

                        def heads(ap, lo, hi):
                            return ap.rearrange("p (h d) -> p h d", h=nh)[:, :, lo:hi]

                        def tab(k, lo, hi):
                            return rot_b[:, k, t, lo:hi].unsqueeze(1).broadcast_to([P, nh, hi - lo])
                        src, m2 = ps_pm[:, b, 0:w], prod[:, (3 * t + i) % 2, 0:w]
                        if i == 2:
                            nc.vector.tensor_copy(qkr[:, t, QB:], ps_pm[:, b, w:])
                        nc.vector.tensor_tensor(heads(qkr[:, t, 512 * i:512 * i + w], 0, DB), heads(src, 0, DB),
                                                tab(0, 0, DB), ALU.mult)
                        nc.vector.tensor_tensor(heads(m2, 0, half), heads(src, half, DB), tab(1, 0, half), ALU.mult)
                        nc.vector.tensor_tensor(heads(m2, half, DB), heads(src, 0, half), tab(1, half, DB),
                                                ALU.mult).then_inc(pm_free[b], 1)

                def split(t):
                    for i in range(3) if "P" in on else ():
                        b = RING_PM_B.bank(s, f"qkT{t}{i}")
                        dve.wait_ge(hi_in, NB + 6 * n + (3 * t + i + 1))
                        cols = slice(P * t, P * (t + 1))
                        src = ps_pm[:, b, :].rearrange("p (j t) -> p j t", j=4)
                        if i < 2:
                            ins = nc.vector.tensor_tensor(qlo[u][:, 4 * i:4 * i + 4, cols], src,
                                                          qhi[u][:, 4 * i:4 * i + 4, cols].bitcast(F32), ALU.subtract)
                        else:
                            for k in range(2):
                                half = slice(DB * k, DB * (k + 1))
                                ins = nc.vector.tensor_tensor(klo[u][half, :, cols], src[half, 0:2],
                                                              kdiag[u][half, :, k, cols].bitcast(F32), ALU.subtract)
                        ins.then_inc(pm_free[b], 1)

                if "P" in on:
                    dve.wait_ge(xs_in, NB + n + 1)
                    mean_square(xs[u], root_p, chain_p, CHAIN_B * n, var_p)
                maxima(0, 2)
                if "T" in on:
                    dve.wait_ge(s_dma, 32 * s)
                    nc.vector.reciprocal(sums[:, :], sums[:, :]).then_inc(inv_sb, 1)
                maxima(2, 4)
                if "P" in on:
                    dve.wait_ge(r0_p, n + 1)
                    newton(root_p, chain_p, CHAIN_B * n + 2)
                    for t in range(NT):
                        ins = nc.vector.scalar_tensor_tensor(xn[:, t, :], xs[u][:, t, :], root_p.r[:, t:t + 1],
                                                             g1b[:, :], ALU.mult, ALU.mult)
                    ins.then_inc(xn_in, 1)
                if "T" in on and draining(s):
                    dve.wait_ge(b_dma, 32 * s)
                    for b in range(2):
                        half = slice(DB * b, DB * (b + 1))
                        for t in range(NT):
                            ins = nc.vector.tensor_tensor(
                                oT[half, t], pvb[1 - u][half, b, t, :, :].rearrange("p k (g c) -> p k g c", g=G),
                                oT[half, t], ALU.mult)
                    ins.then_inc(oT_in, 1)
                maxima(4, 8)
                rotate(0)
                maxima(8, 10)
                if "T" in on:
                    for t in range(NT):
                        b = RING_ST_B.bank(s, f"wo{t}")
                        dve.wait_ge(st_full, RING_ST_B.full(s, f"wo{t}"))
                        nc.vector.tensor_tensor(y[:, t, :], ps_o[:, b, 0:C], tiles(x1_all, m)[:, t, :],
                                                ALU.add).then_inc(st_free[b], 1)
                    for t in range(NT):
                        emptied(dve, RING_ST_B, s, f"wo{t}")
                    nc.vector.tensor_tensor(tiles(z_all, m), tiles(x1_all, m), y[:, :, :], ALU.add).then_inc(z_in, 1)
                    mean_square(y, root_t, chain_t, CHAIN_A * NB + CHAIN_B * m, var_t)
                rotate(1)
                maxima(10, 12)
                if "T" in on:
                    dve.wait_ge(r0_t, NB + m + 1)
                    newton(root_t, chain_t, CHAIN_A * NB + CHAIN_B * m + 2)
                    if some(m):
                        dve.wait_ge(xfa_in, m)
                    for t in range(NT):
                        ins = nc.vector.scalar_tensor_tensor(xf[:, t, :], y[:, t, :], root_t.r[:, t:t + 1],
                                                             g2b[:, :], ALU.mult, ALU.mult)
                    ins.then_inc(xf_in, 1)
                split(0)
                if "T" in on:
                    b = RING_ST_B.bank(s, "lg")
                    dve.wait_ge(st_full, RING_ST_B.full(s, "lg"))
                    nc.vector.tensor_copy(tiles(lg_all, m), ps_o[:, b, 0:NT * E].rearrange("p (t e) -> p t e", t=NT)) \
                        .then_inc(st_free[b], 1)
                split(1)

            dve.wait_ge(wb_in, WB_IN)
            pipeline(dve, step_b)

            def low_tokens(j):
                dve.wait_ge(xgh_in, j + 1)
                nc.vector.tensor_tensor(xgl, xfT_all[:, bass.ds(j * NG, NG)], xgh.bitcast(F32), ALU.subtract) \
                    .then_inc(xgl_in, 1)

            def route():
                at = [0]

                def link(ins):
                    at[0] += 1
                    ins.then_inc(chain_r, 1)
                    dve.wait_ge(chain_r, at[0])

                def per_expert(ap):
                    return ap.unsqueeze(2).broadcast_to([P, NTILES, E])

                def per_tile(ap):
                    return ap.unsqueeze(1).broadcast_to([P, NTILES, E])

                TT, V = nc.vector.tensor_tensor, nc.vector
                last = RING_ST_B.total()
                dve.wait_ge(st_free[last % 2], last // 2)
                dve.wait_ge(st_free[1 - last % 2], (last + 1) // 2)
                src = lg_all
                for k in range(2):
                    link(V.tensor_reduce(top[:, k, :], src[:, :, :], AX.X, ALU.max))
                    link(TT(rt[:, 0], src[:, :, :], per_expert(top[:, k, :]), ALU.is_equal))
                    link(TT(rt[:, 0], rt[:, 0], per_tile(down), ALU.mult))
                    link(V.tensor_reduce(ru[:, 0], rt[:, 0], AX.X, ALU.max))
                    link(TT(oh[:, k], rt[:, 0], per_expert(ru[:, 0]), ALU.is_equal))
                    if k == 0:
                        link(V.scalar_tensor_tensor(rt[:, 1], oh[:, 0], -3e38, lg_all[:, :, :], ALU.mult, ALU.add))
                        src = rt[:, 1]
                link(V.tensor_copy(oh_b[:, :, :, :], oh[:, :, :, :]))
                V.tensor_tensor(ru[:, 1], top[:, 1, :], top[:, 0, :], ALU.subtract).then_inc(oh_in, 1)
                dve.wait_ge(xfa_in, NB)
                low_tokens(0)
                dve.wait_ge(e_in, 1)
                link(V.tensor_scalar(ru[:, 3], ru[:, 2], 1.0, None, ALU.add))
                link(V.reciprocal(score[:, 0], ru[:, 3]))
                link(TT(score[:, 1], ru[:, 2], score[:, 0], ALU.mult))
                dve.wait_ge(cnt_in, 1)
                cnt = ps_o[:, 0, 0:2 * NTILES * E].rearrange("p (k t e) -> p k t e", k=2, t=NTILES)
                link(V.tensor_copy(rt[:, 0], cnt[:, 0]))
                link(TT(rt[:, 1], rt[:, 0], cnt[:, 1], ALU.add))
                for k in range(2):
                    link(V.scalar_tensor_tensor(oh[:, k], rt[:, k], float(CAP), oh[:, k], ALU.is_lt, ALU.mult))
                    link(V.tensor_reduce(fits[:, k], oh[:, k], AX.X, ALU.add))
                    link(TT(rt[:, k], oh[:, k], per_tile(iota), ALU.mult))
                    link(V.tensor_reduce(ru[:, k], rt[:, k], AX.X, ALU.max))
                link(TT(ru[:, 0], ru[:, 0], ru[:, 1], ALU.max))
                link(TT(fits[:, :], fits[:, :], score[:, :], ALU.mult))
                link(TT(score[:, :], score[:, :], fits[:, :], ALU.subtract))
                link(TT(wx[:, :], score[:, 0], score[:, 1], ALU.add))
                link(TT(ru[:, 1], fits[:, 0], fits[:, 1], ALU.add))
                link(TT(rt[:, 0], per_tile(iota), per_expert(ru[:, 0]), ALU.is_equal))
                link(TT(we[:, :, :], rt[:, 0], per_expert(ru[:, 1]), ALU.mult))

            def layernorm(j, piece):
                V, TT = nc.vector, nc.vector.tensor_tensor
                c0 = j * CHAIN_F
                k = [2 * GT]
                final = z_all[:, bass.ds(j * GT, GT), :]
                fv, fa, fr = froot[:, 0, :], froot[:, 1, :], froot[:, 2, :]

                def link(ins):
                    k[0] += 1
                    ins.then_inc(chain_f, 1)
                    dve.wait_ge(chain_f, c0 + k[0])
                if piece == 0:
                    for t in range(GT):
                        V.bn_stats(fstat[:, t, :], final[:, t, :]).then_inc(chain_f, 1)
                    dve.wait_ge(chain_f, c0 + GT)
                    nc.vector.memset(carrier[:, :], 0.0)
                    for t in range(GT):
                        V.bn_aggr(fmv[:, t, :], fstat[:, t, :]).then_inc(chain_f, 1)
                if piece == 1:
                    I32 = mybir.dt.int32
                    dve.wait_ge(chain_f, c0 + 2 * GT)
                    link(V.tensor_scalar(fv, fmv[:, :, 1], EPS_LN, None, ALU.add))
                    link(V.tensor_scalar(fa.bitcast(I32), fv.bitcast(I32), 1, None, ALU.logical_shift_right))
                    link(V.tensor_scalar(fr.bitcast(I32), fa.bitcast(I32), -1, 0x5f3759df, ALU.mult, ALU.add))
                    for _ in range(3):
                        link(TT(fa, fr, fr, ALU.mult))
                        link(TT(fa, fa, fv, ALU.mult))
                        link(V.tensor_scalar(fa, fa, -0.5, 1.5, ALU.mult, ALU.add))
                        link(TT(fr, fr, fa, ALU.mult))
                    assert k[0] == CHAIN_F
                if piece == 2:
                    for t in range(GT):
                        ins = V.tensor_scalar(final[:, t, :], final[:, t, :], fmv[:, t, 0:1], fr[:, t:t + 1],
                                              ALU.subtract, ALU.mult)
                    ins.then_inc(fin_in, 1)

            def group(j):
                gt = bass.ds(j * GT, GT)
                acc = z_all[:, gt, :]

                def gate(e):
                    for k in range(HK):
                        i = HK * e + k
                        dve.wait_ge(a_in, j * (E * HK) + (i + 1))
                        nc.vector.tensor_tensor(gated[:, i % 2, :], asb[:, i % 2, :], ps_st[:, i % 2, 1, :],
                                                ALU.mult).then_inc(prod_e, 1)

                def add(e):
                    dve.wait_ge(down_full, j * E + (e + 1))
                    if e:
                        dve.wait_ge(acc_in, j * E + e)
                    for t in range(GT):
                        ins = nc.vector.scalar_tensor_tensor(acc[:, t, :], ps_pm[:, e % 2, C * t:C * (t + 1)],
                                                             weg[:, t, e:e + 1], acc[:, t, :], ALU.mult, ALU.add)
                    ins.then_inc(acc_in, 1)

                gate(0)
                if some(j):
                    dve.wait_ge(acc_in, j * E)
                for t in range(GT):
                    nc.vector.scalar_tensor_tensor(acc[:, t, :], xf_all[:, gt, :][:, t, :], wx[:, gt][:, t:t + 1],
                                                   acc[:, t, :], ALU.mult, ALU.add).then_inc(acc0_in, 1)
                nc.vector.tensor_copy(weg[:, :, :], we[:, gt, :]).then_inc(acc0_in, 1)
                dve.wait_ge(acc0_in, (GT + 1) * (j + 1))
                for e in range(E):
                    if e + 1 < E:
                        gate(e + 1)
                    if some(j) and 1 <= e <= 3:
                        layernorm(j - 1, e - 1)
                    if e + 2 == E and another(j):
                        low_tokens(j + 1)
                    add(e)


            route()
            groups(dve, group)
            dve.wait_ge(acc_in, NGROUPS * E)
            for piece in range(3):
                layernorm(NGROUPS - 1, piece)

        @block.scalar
        def _(act):
            nc.scalar.dma_start(x_all[:, 0:NT, :], x[0].rearrange("(t p) c -> p t c", p=P)).then_inc(x0_in, 16)
            nc.scalar.dma_start(x_all[:, NT:, :], x[1:].rearrange("b (t p) c -> p (b t) c", p=P)).then_inc(x_in, 16)
            for to, of in ((wqkv[:, 0:H * DB], wq), (wqkv[:, H * DB:QB], wk), (wqkv[:, QB:], wv),
                           (rw[:, :], router_w), (rb[:, :], router_b[None, :]),
                           (g1b[:, :], g1[None, :].broadcast_to([P, C])),
                           (g2b[:, :], g2[None, :].broadcast_to([P, C])),
                           (wob[:, :, :], wo.rearrange("(j p) c -> p j c", p=P))):
                nc.scalar.dma_start(to, of).then_inc(wb_in, 16)
            nc.scalar.preload_act_table_set("natural_log_exp_and_others")

            def exp_chunk(count, c, scale):
                kind, half = CHUNKS[c]
                act.wait_ge(sc_full, count * NCH + (c + 1))
                nc.scalar.activation(pt[:, kind, 8 * half:8 * half + 8, :],
                                     ps_st[:, c % 2, :, :].rearrange("p b (h t) -> p (b h) t", h=4),
                                     ACT.Exp, scale=scale).then_inc(probs, 1)

            def neg_max(ring, s, count):
                b = ring.bank(s, "nmT")
                act.wait_ge(pm_full, ring.full(s, "nmT"))
                if some(count):
                    act.wait_ge(n_dma, 32 * count)
                nc.scalar.activation(negmax[:, :], ps_pm[0:NT * H, b, 0:P], ACT.Copy, scale=-1.0) \
                    .then_inc(pm_free[b], 1)

            def turned_x(ring, s, u):
                b = ring.bank(s, "xT")
                act.wait_ge(pm_full, ring.full(s, "xT"))
                nc.scalar.activation(xT[u][:, :], ps_pm[:, b, 0:T], ACT.Copy).then_inc(pm_free[b], 1)

            def inverse_root(root, var, ln, r0, count):
                act.wait_ge(var, count)
                nc.scalar.activation(root.ln[:, :], root.v[:, :], ACT.Ln).then_inc(ln, 1)
                act.wait_ge(ln, count)
                nc.scalar.activation(root.r0[:, :], root.ln[:, :], ACT.Exp, scale=-0.5).then_inc(r0, 1)

            def step_a(s, u, on):
                n, m = s + 2, s - 1

                def high_parts():
                    if "P" in on:
                        b = RING_PM_A.bank(s, "qT")
                        act.wait_ge(pm_full, RING_PM_A.full(s, "qT"))
                        if some(n):
                            act.wait_ge(q_dma, 48 * n)
                        nc.scalar.activation(qh[:, :], ps_pm[:, b, 0:T], ACT.Copy).then_inc(hi_in, 1)
                        for i in range(2):
                            b = RING_PM_A.bank(s, f"kT{i}")
                            act.wait_ge(pm_full, RING_PM_A.full(s, f"kT{i}"))
                            nc.scalar.activation(k96[u][:, 2 * i:2 * i + 2, :],
                                                 ps_pm[0:R96, b, :].rearrange("p (a t) -> p a t", a=2),
                                                 ACT.Copy).then_inc(pm_free[b], 1)

                def take_values(qt):
                    if "S" in on:
                        b = RING_ST_A.bank(s, f"pv{qt}")
                        act.wait_ge(st_full, RING_ST_A.full(s, f"pv{qt}"))
                        if qt == 0 and "T" in on:
                            act.wait_ge(o_dma, 64 * s)
                        nc.scalar.activation(pvs[:, qt, :], ps_o[0:8 * DA, b, :], ACT.Copy).then_inc(st_free[b], 1)

                def exp(c):
                    if "S" in on:
                        exp_chunk(s, c, DA ** -0.5)

                if "P" in on:
                    turned_x(RING_PM_A, s, u)
                exp(0)
                exp(1)
                take_values(0)
                exp(2)
                exp(3)
                exp(4)
                if "T" in on:
                    inverse_root(root_t, var_t, ln_t, r0_t, m + 1)
                exp(5)
                if "M" in on:
                    neg_max(RING_PM_A, s, s + 1)
                high_parts()
                take_values(1)

            pipeline(act, step_a)

            def step_b(s, u, on):
                n, m = s + 2, s - 1

                def exp(c):
                    if "S" in on:
                        exp_chunk(s + NB, c, DB ** -0.5)

                def take_values(lo, hi):
                    for i in range(lo, hi) if "S" in on else ():
                        b = RING_ST_B.bank(s, f"pv{i}")
                        act.wait_ge(st_full, RING_ST_B.full(s, f"pv{i}"))
                        if i == 0 and some(s - 1):
                            act.wait_ge(oT_in, NB + s - 1)
                        qt, hk = i // HKV, i % HKV
                        nc.scalar.activation(pvb[u][:, hk % 2, qt, hk // 2, :], ps_o[:, b, :], ACT.Copy) \
                            .then_inc(st_free[b], 1)

                def high_parts(t):
                    for i in range(3) if "P" in on else ():
                        b = RING_PM_B.bank(s, f"qkT{t}{i}")
                        act.wait_ge(pm_full, RING_PM_B.full(s, f"qkT{t}{i}"))
                        src = ps_pm[:, b, :].rearrange("p (j t) -> p j t", j=4)
                        cols = slice(P * t, P * (t + 1))
                        if i < 2:
                            ins = nc.scalar.activation(qhi[u][:, 4 * i:4 * i + 4, cols], src, ACT.Copy)
                        else:
                            for k in range(2):
                                half = slice(DB * k, DB * (k + 1))
                                ins = nc.scalar.activation(kdiag[u][half, :, k, cols], src[half, 0:2], ACT.Copy)
                        ins.then_inc(hi_in, 1)

                exp(0)
                if "P" in on:
                    inverse_root(root_p, var_p, ln_p, r0_p, n + 1)
                exp(1)
                take_values(0, 2)
                if "P" in on:
                    turned_x(RING_PM_B, s, u)
                exp(2)
                take_values(2, 4)
                exp(3)
                take_values(4, 6)
                exp(4)
                if "T" in on:
                    inverse_root(root_t, var_t, ln_t, r0_t, NB + m + 1)
                exp(5)
                if "M" in on:
                    neg_max(RING_PM_B, s, NB + s + 1)
                take_values(6, 8)
                if "T" in on:
                    b = RING_ST_B.bank(s, "xfT")
                    act.wait_ge(st_full, RING_ST_B.full(s, "xfT"))
                    if some(m):
                        act.wait_ge(xfa_in, m)
                    nc.scalar.activation(xfT[:, :], ps_o[:, b, 0:T], ACT.Copy).then_inc(st_free[b], 1)
                high_parts(0)
                high_parts(1)

            act.wait_ge(zeroed, 5)
            pipeline(act, step_b)

            def high_tokens(j):
                nc.scalar.activation(xgh, xfT_all[:, bass.ds(j * NG, NG)], ACT.Copy).then_inc(xgh_in, 1)

            def group(j):
                def copy(i):
                    act.wait_ge(up_full, j * (E * HK) + (i + 1))
                    need = j * (E * HK) + (i - 1)
                    if some(need):
                        act.wait_ge(prod_e, need)
                    nc.scalar.activation(asb[:, i % 2, :], ps_st[:, i % 2, 0, :], ACT.Copy).then_inc(a_in, 1)

                def gelu(i):
                    act.wait_ge(prod_e, j * (E * HK) + (i + 1))
                    need = j * E + (i // HK - 1)
                    if i % HK == 0 and some(need):
                        act.wait_ge(down_full, need)
                    nc.scalar.activation(hid[:, i // HK % 2, i % HK, :], gated[:, i % 2, :], ACT.Gelu).then_inc(hid_in, 1)

                copy(0)
                for i in range(E * HK):
                    if i + 1 < E * HK:
                        copy(i + 1)
                    if i + 2 == E * HK and another(j):
                        high_tokens(j + 1)
                    gelu(i)

            act.wait_ge(w12_in, 32)
            for e in range(0, E, 2):
                for w in range(2):
                    nc.scalar.activation(w12h[:, w, e:e + 2, :], (w1s, w2s)[w][:, e:e + 2, :], ACT.Copy) \
                        .then_inc(wh_in, 1)
            act.wait_ge(xfa_in, NB)
            high_tokens(0)
            act.wait_ge(oh_in, 1)
            nc.scalar.activation(ru[:, 2], ru[:, 1], ACT.Exp).then_inc(e_in, 1)
            nc.scalar.preload_act_table_set("gelu_and_others")
            groups(act, group)


_NAMES = ["L0_attn_x", "L0_attn_Wq", "L0_attn_bq", "L0_attn_Wk", "L0_attn_bk", "L0_attn_Wv", "L0_attn_bv",
          "L0_attn_Wo", "L0_attn_bo", "L0_ffn_g1", "L0_ffn_g2", "L0_ffn_wq", "L0_ffn_wk", "L0_ffn_wv",
          "L0_ffn_wo", "L0_ffn_router_w", "L0_ffn_router_b", "L0_ffn_w1", "L0_ffn_w2", "L0_ffn_w3"]


def kernel(**inputs):
    import concourse.bacc as bacc
    from concourse.bass_utils import run_bass_kernel_spmd

    nc = bacc.Bacc("TRN2", target_bir_lowering=False, num_devices=1)
    arrays, args = {}, []
    cf, cb = consts()
    for name, a in [(n, inputs[n]) for n in _NAMES] + [("table_f32", cf), ("table_bf16", cb)]:
        a = np.ascontiguousarray(a)
        arrays[f"in_{name}"] = a
        args.append(nc.dram_tensor(f"in_{name}", a.shape, mybir.dt.from_np(a.dtype), kind="ExternalInput").ap())
    args.append(nc.dram_tensor("out_0", (NB, T, C), F32, kind="ExternalOutput").ap())
    build(nc, *args)
    r = run_bass_kernel_spmd(nc, [arrays], core_ids=[0])
    return r.results[0]["out_0"]
```
